# Optimizing a Trainium2 kernel written in Bass

```python
import numpy as np
import jax
import jax.numpy as jnp

def _softmax(x, axis=-1):
    return jax.nn.softmax(x, axis=axis)

def _gelu(x):
    return jax.nn.gelu(x, approximate=True)

def _silu(x):
    return jax.nn.silu(x)

def _sigmoid(x):
    return jax.nn.sigmoid(x)

def _layernorm(x, axis=-1, eps=1e-05):
    m = jnp.mean(x, axis=axis, keepdims=True)
    v = jnp.var(x, axis=axis, keepdims=True)
    return (x - m) / jnp.sqrt(v + eps)

def _scatter_add(tgt, idx, src, axis=0):
    return tgt.at[idx].add(src)

def _segment_sum(src, seg, n):
    return jax.ops.segment_sum(src, seg, n)
kernel_name = 'mk_dlrm_tower_d1_rec_r8_abb456'

def setup_inputs(seed: int=0):
    np.random.seed(seed)
    _w = jnp.asarray

    def _rec_inputs():
        import jax
        import jax.numpy as jnp
        _tk = jax.random.key(seed)
        ids = jnp.stack([jax.random.randint(jax.random.fold_in(_tk, 200 + f), (2048,), 0, v, jnp.int32) for f, v in enumerate([1250, 125000, 1000, 1000, 12500, 1250, 12500, 12500, 1250, 1250, 12500, 12500, 1250, 12500, 1000, 1000, 12500, 1000, 12500, 1250, 1250, 1250, 1000, 1000, 1250, 1000])], axis=1)
        tbl_0 = 0.05 * jax.random.normal(jax.random.fold_in(_tk, 500 + 0), (1250, 128), jnp.float32)
        tbl_1 = 0.05 * jax.random.normal(jax.random.fold_in(_tk, 500 + 1), (125000, 128), jnp.float32)
        tbl_2 = 0.05 * jax.random.normal(jax.random.fold_in(_tk, 500 + 2), (1000, 128), jnp.float32)
        tbl_3 = 0.05 * jax.random.normal(jax.random.fold_in(_tk, 500 + 3), (1000, 128), jnp.float32)
        tbl_4 = 0.05 * jax.random.normal(jax.random.fold_in(_tk, 500 + 4), (12500, 128), jnp.float32)
        tbl_5 = 0.05 * jax.random.normal(jax.random.fold_in(_tk, 500 + 5), (1250, 128), jnp.float32)
        tbl_6 = 0.05 * jax.random.normal(jax.random.fold_in(_tk, 500 + 6), (12500, 128), jnp.float32)
        tbl_7 = 0.05 * jax.random.normal(jax.random.fold_in(_tk, 500 + 7), (12500, 128), jnp.float32)
        tbl_8 = 0.05 * jax.random.normal(jax.random.fold_in(_tk, 500 + 8), (1250, 128), jnp.float32)
        tbl_9 = 0.05 * jax.random.normal(jax.random.fold_in(_tk, 500 + 9), (1250, 128), jnp.float32)
        tbl_10 = 0.05 * jax.random.normal(jax.random.fold_in(_tk, 500 + 10), (12500, 128), jnp.float32)
        tbl_11 = 0.05 * jax.random.normal(jax.random.fold_in(_tk, 500 + 11), (12500, 128), jnp.float32)
        tbl_12 = 0.05 * jax.random.normal(jax.random.fold_in(_tk, 500 + 12), (1250, 128), jnp.float32)
        tbl_13 = 0.05 * jax.random.normal(jax.random.fold_in(_tk, 500 + 13), (12500, 128), jnp.float32)
        tbl_14 = 0.05 * jax.random.normal(jax.random.fold_in(_tk, 500 + 14), (1000, 128), jnp.float32)
        tbl_15 = 0.05 * jax.random.normal(jax.random.fold_in(_tk, 500 + 15), (1000, 128), jnp.float32)
        tbl_16 = 0.05 * jax.random.normal(jax.random.fold_in(_tk, 500 + 16), (12500, 128), jnp.float32)
        tbl_17 = 0.05 * jax.random.normal(jax.random.fold_in(_tk, 500 + 17), (1000, 128), jnp.float32)
        tbl_18 = 0.05 * jax.random.normal(jax.random.fold_in(_tk, 500 + 18), (12500, 128), jnp.float32)
        tbl_19 = 0.05 * jax.random.normal(jax.random.fold_in(_tk, 500 + 19), (1250, 128), jnp.float32)
        tbl_20 = 0.05 * jax.random.normal(jax.random.fold_in(_tk, 500 + 20), (1250, 128), jnp.float32)
        tbl_21 = 0.05 * jax.random.normal(jax.random.fold_in(_tk, 500 + 21), (1250, 128), jnp.float32)
        tbl_22 = 0.05 * jax.random.normal(jax.random.fold_in(_tk, 500 + 22), (1000, 128), jnp.float32)
        tbl_23 = 0.05 * jax.random.normal(jax.random.fold_in(_tk, 500 + 23), (1000, 128), jnp.float32)
        tbl_24 = 0.05 * jax.random.normal(jax.random.fold_in(_tk, 500 + 24), (1250, 128), jnp.float32)
        tbl_25 = 0.05 * jax.random.normal(jax.random.fold_in(_tk, 500 + 25), (1000, 128), jnp.float32)
        _rk = jax.random.fold_in(_tk, 7)
        r_dense_x = -0.000514642 + 1.00011 * jax.random.normal(jax.random.fold_in(_rk, 101), (2048, 128), jnp.float32)
        W_top1 = 0.0456912 * jax.random.normal(jax.random.fold_in(_tk, 801), (479, 512), jnp.float32)
        W_top2 = 0.0441942 * jax.random.normal(jax.random.fold_in(_tk, 802), (512, 256), jnp.float32)
        W_top3 = 0.0625 * jax.random.normal(jax.random.fold_in(_tk, 803), (256, 1), jnp.float32)
        b_top1 = jnp.zeros((512,), jnp.float32)
        b_top2 = jnp.zeros((256,), jnp.float32)
        return (r_dense_x, ids, tbl_0, tbl_1, tbl_2, tbl_3, tbl_4, tbl_5, tbl_6, tbl_7, tbl_8, tbl_9, tbl_10, tbl_11, tbl_12, tbl_13, tbl_14, tbl_15, tbl_16, tbl_17, tbl_18, tbl_19, tbl_20, tbl_21, tbl_22, tbl_23, tbl_24, tbl_25, W_top1, b_top1, W_top2, b_top2, W_top3)
    r_dense_x, ids, tbl_0, tbl_1, tbl_2, tbl_3, tbl_4, tbl_5, tbl_6, tbl_7, tbl_8, tbl_9, tbl_10, tbl_11, tbl_12, tbl_13, tbl_14, tbl_15, tbl_16, tbl_17, tbl_18, tbl_19, tbl_20, tbl_21, tbl_22, tbl_23, tbl_24, tbl_25, W_top1, b_top1, W_top2, b_top2, W_top3 = _rec_inputs()

    def _L0_rec_setup():
        import jax, jax.numpy as jnp
        import numpy as np
        F = 26
        D = 128
        B = 2048
        _TRIU_I, _TRIU_J = np.triu_indices(F + 1, k=1)
        _TRIU_I = jnp.asarray(_TRIU_I)
        _TRIU_J = jnp.asarray(_TRIU_J)
        key = jax.random.key(seed)
        k1, k2 = jax.random.split(key)
        sparse_x = jax.random.normal(k1, (B, F, D), dtype=jnp.float32)
        dense_x = jax.random.normal(k2, (B, D), dtype=jnp.float32)
        return {'sparse_x': sparse_x, 'dense_x': dense_x}
    _L0_rec_all = _L0_rec_setup()
    _L0_rec_in = {k: v for k, v in _L0_rec_all.items() if k in ()}
    del _L0_rec_all
    return {'r_dense_x': r_dense_x, 'ids': ids, 'tbl_0': tbl_0, 'tbl_1': tbl_1, 'tbl_2': tbl_2, 'tbl_3': tbl_3, 'tbl_4': tbl_4, 'tbl_5': tbl_5, 'tbl_6': tbl_6, 'tbl_7': tbl_7, 'tbl_8': tbl_8, 'tbl_9': tbl_9, 'tbl_10': tbl_10, 'tbl_11': tbl_11, 'tbl_12': tbl_12, 'tbl_13': tbl_13, 'tbl_14': tbl_14, 'tbl_15': tbl_15, 'tbl_16': tbl_16, 'tbl_17': tbl_17, 'tbl_18': tbl_18, 'tbl_19': tbl_19, 'tbl_20': tbl_20, 'tbl_21': tbl_21, 'tbl_22': tbl_22, 'tbl_23': tbl_23, 'tbl_24': tbl_24, 'tbl_25': tbl_25, 'W_top1': W_top1, 'b_top1': b_top1, 'W_top2': W_top2, 'b_top2': b_top2, 'W_top3': W_top3}

def reference(r_dense_x, ids, tbl_0, tbl_1, tbl_2, tbl_3, tbl_4, tbl_5, tbl_6, tbl_7, tbl_8, tbl_9, tbl_10, tbl_11, tbl_12, tbl_13, tbl_14, tbl_15, tbl_16, tbl_17, tbl_18, tbl_19, tbl_20, tbl_21, tbl_22, tbl_23, tbl_24, tbl_25, W_top1, b_top1, W_top2, b_top2, W_top3):
    import jax
    import jax.numpy as jnp

    def _L0_rec_ref(sparse_x, dense_x):
        import jax, jax.numpy as jnp
        import numpy as np
        F = 26
        D = 128
        B = 2048
        _TRIU_I, _TRIU_J = np.triu_indices(F + 1, k=1)
        _TRIU_I = jnp.asarray(_TRIU_I)
        _TRIU_J = jnp.asarray(_TRIU_J)
        combined = jnp.concatenate([sparse_x, dense_x[:, None, :]], axis=1)
        interact = jnp.einsum('bfd,bgd->bfg', combined, combined)
        return interact[:, _TRIU_I, _TRIU_J]
    e = jnp.stack([tbl_0[ids[:, 0]], tbl_1[ids[:, 1]], tbl_2[ids[:, 2]], tbl_3[ids[:, 3]], tbl_4[ids[:, 4]], tbl_5[ids[:, 5]], tbl_6[ids[:, 6]], tbl_7[ids[:, 7]], tbl_8[ids[:, 8]], tbl_9[ids[:, 9]], tbl_10[ids[:, 10]], tbl_11[ids[:, 11]], tbl_12[ids[:, 12]], tbl_13[ids[:, 13]], tbl_14[ids[:, 14]], tbl_15[ids[:, 15]], tbl_16[ids[:, 16]], tbl_17[ids[:, 17]], tbl_18[ids[:, 18]], tbl_19[ids[:, 19]], tbl_20[ids[:, 20]], tbl_21[ids[:, 21]], tbl_22[ids[:, 22]], tbl_23[ids[:, 23]], tbl_24[ids[:, 24]], tbl_25[ids[:, 25]]], axis=1)
    z = _L0_rec_ref(e, r_dense_x)
    z = z.reshape(z.shape[0], -1)
    h = jnp.concatenate([z, r_dense_x], axis=1)
    h = jnp.maximum(h @ W_top1 + b_top1, 0.0)
    h = jnp.maximum(h @ W_top2 + b_top2, 0.0)
    y = h @ W_top3
    return y

_drawn_inputs = setup_inputs


def setup_inputs(seed=0):
    import zlib

    import numpy as np

    out = dict(_drawn_inputs(seed))
    spreads = {'b_top1': (0.0, 0.1), 'b_top2': (0.0, 0.1)}
    factors = {}
    for name, (base, spread) in spreads.items():
        noise = np.random.default_rng([zlib.crc32(name.encode()), seed]).standard_normal(out[name].shape)
        drawn = base * np.exp(spread * noise) if base else spread * noise
        out[name] = jnp.asarray(drawn.astype(out[name].dtype))
    for name, factor in factors.items():
        out[name] = (out[name] * factor).astype(out[name].dtype)
    return out
```

```python
from contextlib import ExitStack

import numpy as np

import concourse.bass as bass
from concourse import mybir

F32 = mybir.dt.float32
I32 = mybir.dt.int32
ALU = mybir.AluOpType
ACT = mybir.ActivationFunctionType

P = 128
D = 128
TABLES = 26
F = TABLES + 1
FPAD = 32
HID1, HID2 = 512, 256

COLS = 7
COL0 = [0, 7, 14, F - COLS]
CHUNKS = COLS + 1
GROUP = 4
BATCH = 8
BATCHES = P // GROUP // BATCH
HALF = 2 * P
TURNS = 7


ROWS_IN = 64


def turn_features(n):
    return range(4 * n, min(4 * n + 4, TABLES))


def bass_dlrm_tower(nc, denseT, ids, tables, w1, b1, w2, b2, w3, out):
    B = ids.shape[0]
    TILES = B // P
    LOOPS = TILES // 4

    with ExitStack() as ctx:
        def sb(name, shape, dt=F32):
            return ctx.enter_context(nc.sbuf_tensor(name, shape, dt))

        def pb(name, shape):
            return ctx.enter_context(nc.psum_tensor(name, shape, F32))

        def sem(name):
            return ctx.enter_context(nc.semaphore(name))

        ident = sb("ident", [P, P])
        ids_now = sb("ids_now", [P, 4, TABLES], I32)
        nought, turnstile = sb("nought", [P, 1]), sb("turnstile", [P, 4])
        rows = sb("rows", [P, 4, TABLES, D])
        dense_half = sb("dense_half", [P, 2, HALF])
        feat = [sb(f"feat{i}", [P, P, FPAD]) for i in range(2)]
        z = [sb(f"z{i}", [P, COLS, HALF]) for i in range(2)]
        w1_sb = sb("w1_sb", [P, CHUNKS, HID1])
        w2_sb = sb("w2_sb", [P, HID1 // P, HID2])
        w3_sb = sb("w3_sb", [P, HID2 // P])
        b1_sb = sb("b1_sb", [P, HID1 // P])
        b2_sb = sb("b2_sb", [P, HID2 // P])
        hid1 = sb("hid1", [P, HID1 // P, HALF])
        hid2 = sb("hid2", [P, HID2 // P, HALF])
        y = sb("y", [1, B])

        ps_turn = [pb(f"ps_turn{i}", [P, 4, P]) for i in range(2)]
        ps_gram = [pb(f"ps_gram{i}", [P, BATCH, P]) for i in range(2)]
        ps_mlp = [pb(f"ps_mlp{i}", [P, 512]) for i in range(2)]

        ident_zero = sem("ident_zero")
        ident_ready = sem("ident_ready")
        pads_ready = sem("pads_ready")
        weights_landed = sem("weights_landed")
        ids_landed = [sem(f"ids_landed{r}") for r in range(4)]
        rows_landed = [[sem(f"rows_landed{r}_{n}") for n in range(TURNS)] for r in range(4)]
        dense_landed = [sem(f"dense_landed{h}") for h in range(2)]
        passed = sem("passed")
        turned = sem("turned")
        feat_copied = [sem("feat_copied_act"), sem("feat_copied_dve")]
        dense_copied = sem("dense_copied")
        gram_done = sem("gram_done")
        z_copied = [sem("z_copied_act"), sem("z_copied_dve")]
        mlp_done = sem("mlp_done")
        mlp_copied = sem("mlp_copied")
        y_stored = sem("y_stored")

        block = ctx.enter_context(nc.Block())

        MLP_OUTS = HID1 // P + HID2 // P + 1

        @block.sync
        def _(sp):
            def load_ids(at, r):
                return sp.dma_start(ids_now[:, r, :], ids[bass.ds(at, P), :]).then_inc(ids_landed[r], 16)

            def load_dense(at, h):
                sp.dma_start(dense_half[:, h, :], denseT[:, bass.ds(at, HALF)]
                             ).then_inc(dense_landed[h], 16)

            for r in range(4):
                load_ids(P * r, r)
            for h in range(2):
                load_dense(HALF * h, h)
            sp.dma_start(w1_sb[:], w1).then_inc(weights_landed, 16)
            sp.dma_start(w2_sb[:], w2.rearrange("(k p) m -> p k m", p=P)).then_inc(weights_landed, 16)
            sp.dma_start(w3_sb[:], w3).then_inc(weights_landed, 16)
            sp.dma_start(b1_sb[:], b1).then_inc(weights_landed, 16)
            sp.dma_start(b2_sb[:], b2).then_inc(weights_landed, 16)
            with sp.Fori(1, LOOPS) as i:
                for r in range(4):
                    for n in range(TURNS):
                        sp.wait_ge(rows_landed[r][n], ROWS_IN * i)
                    load_ids((4 * i + r) * P, r)
                    if r % 2:
                        sp.wait_ge(mlp_done, MLP_OUTS * (2 * i - 1 + r // 2))
                        load_dense((2 * i + r // 2) * HALF, r // 2)
            sp.wait_ge(mlp_copied, MLP_OUTS * 2 * LOOPS)
            sp.dma_start(out.rearrange("b o -> o b"), y[:]).then_inc(y_stored, 16)
            sp.wait_ge(y_stored, 16)

        @block.gpsimd
        def _(pool):
            def gather(i, r):
                pool.wait_ge(ids_landed[r], 16 * (i + 1))
                nc.gpsimd.tensor_tensor(turnstile[:, r:r + 1], nought[:], nought[:], ALU.add).then_inc(passed, 1)
                for n in range(TURNS):
                    for f in turn_features(n):
                        nc.gpsimd.indirect_dma_start(
                            rows[:, r, f, :], None, tables[f],
                            bass.IndirectOffsetOnAxis(ap=ids_now[:, r, f:f + 1], axis=0),
                        ).then_inc(rows_landed[r][n], ROWS_IN // len(turn_features(n)))

            pool.wait_ge(ident_zero, 2)
            nc.gpsimd.affine_select(out=ident[:], in_=ident[:], compare_op=ALU.not_equal, fill=1.0, base=0,
                                    pattern=[[-1, P]], channel_multiplier=1).then_inc(ident_ready, 1)
            for r in range(4):
                gather(0, r)
            with pool.Fori(1, LOOPS) as i:
                for r in range(4):
                    pool.wait_ge(turned, TURNS * (4 * i + r - 3))
                    pool.wait_ge(passed, 4 * i + r)
                    gather(i, r)

        @block.tensor
        def _(pe):
            def turn(i, r):
                for n in range(TURNS):
                    k = TURNS * r + n
                    pe.wait_ge(rows_landed[r % 4][n], ROWS_IN * (i + r // 4 + 1))
                    if k >= 2 or not isinstance(i, int) or i > 0:
                        pe.wait_ge(feat_copied[k % 2], TURNS * 2 * i + k // 2)
                    for f in turn_features(n):
                        mm = nc.tensor.transpose(ps_turn[k % 2][:, f % 4, :], rows[:, r % 4, f, :], ident[:])
                    mm.then_inc(turned, 1)

            def products(i, r):
                k = TURNS * (r + 1)
                for e in range(2):
                    pe.wait_ge(feat_copied[e], TURNS * 2 * i + (k + 1 - e) // 2)
                pe.wait_ge(dense_copied, 4 * i + r + 1)
                x = feat[r % 2]
                for m in range(BATCHES):
                    b = BATCHES * r + m
                    if b >= 2 or not isinstance(i, int) or i > 0:
                        pe.wait_ge(z_copied[b % 2], BATCHES * 2 * i + b // 2)
                    for c in range(BATCH):
                        s = GROUP * (BATCH * m + c)
                        mm = nc.tensor.matmul(
                            ps_gram[b % 2][:, c, 0:GROUP * F],
                            x[:, s:s + GROUP, :].rearrange("d s f -> d (s f)"),
                            x[:, s:s + GROUP, 0:F], start=True, stop=True)
                    mm.then_inc(gram_done, 1)

            def mlp(i, a):
                for e in range(2):
                    pe.wait_ge(z_copied[e], BATCHES // 2 * (4 * i + 2 * a + 2))
                u = MLP_OUTS * a
                base = MLP_OUTS * 2 * i

                for n in range(HID1 // P):
                    if n >= 2:
                        pe.wait_ge(mlp_copied, base + u + n - 1)
                    for c in range(CHUNKS):
                        x = z[a % 2][:, c, :] if c < COLS else dense_half[:, a % 2, :]
                        mm = nc.tensor.matmul(ps_mlp[(u + n) % 2][:, 0:HALF], w1_sb[:, c, n * P:(n + 1) * P], x,
                                              start=(c == 0), stop=(c == CHUNKS - 1))
                    mm.then_inc(mlp_done, 1)
                u += HID1 // P
                pe.wait_ge(mlp_copied, base + u)
                for n in range(HID2 // P):
                    for c in range(HID1 // P):
                        mm = nc.tensor.matmul(ps_mlp[(u + n) % 2][:, 0:HALF], w2_sb[:, c, n * P:(n + 1) * P],
                                              hid1[:, c, :], start=(c == 0), stop=(c == HID1 // P - 1))
                    mm.then_inc(mlp_done, 1)
                u += HID2 // P
                pe.wait_ge(mlp_copied, base + u)
                for c in range(HID2 // P):
                    mm = nc.tensor.matmul(ps_mlp[u % 2][0:1, 0:HALF], w3_sb[:, c:c + 1], hid2[:, c, :],
                                          start=(c == 0), stop=(c == HID2 // P - 1))
                mm.then_inc(mlp_done, 1)

            pe.wait_ge(ident_ready, 1)
            turn(0, 0)
            turn(0, 1)
            products(0, 0)
            turn(0, 2)
            products(0, 1)
            pe.wait_ge(weights_landed, 16 * 5)
            with pe.Fori(0, LOOPS - 1) as i:
                turn(i, 3)
                products(i, 2)
                mlp(i, 0)
                turn(i, 4)
                products(i, 3)
                turn(i, 5)
                products(i, 4)
                mlp(i, 1)
                turn(i, 6)
                products(i, 5)
            last = LOOPS - 1
            turn(last, 3)
            products(last, 2)
            mlp(last, 0)
            products(last, 3)
            mlp(last, 1)

        def copy_features(eng, copy, e, i, r):
            for n in range(TURNS):
                k = TURNS * r + n
                if k % 2 == e:
                    fs = turn_features(n)
                    eng.wait_ge(turned, TURNS * 4 * i + k + 1)
                    copy(feat[r % 2][:, :, fs[0]:fs[-1] + 1].rearrange("d s f -> d f s"),
                         ps_turn[k % 2][:, 0:len(fs), :]).then_inc(feat_copied[e], 1)

        def copy_products(eng, copy, e, i, r):
            for m in range(e, BATCHES, 2):
                b = BATCHES * r + m
                eng.wait_ge(gram_done, BATCHES * 4 * i + b + 1)
                for j in range(GROUP):
                    for q in range(4):
                        s = P * (r % 2) + GROUP * BATCH * m
                        at = F * j + COL0[q]
                        last = copy(
                            z[r // 2 % 2][32 * q:32 * q + 32, :, s + j:s + GROUP * BATCH:GROUP],
                            ps_gram[b % 2][32 * j:32 * j + 32, :, at:at + COLS].rearrange("p b c -> p c b"))
                last.then_inc(z_copied[e], 1)

        @block.scalar
        def _(act):
            copy = nc.scalar.copy

            def mlp_results(i, a):
                u = MLP_OUTS * (2 * i + a)
                for n in range(HID1 // P):
                    act.wait_ge(mlp_done, u + n + 1)
                    nc.scalar.activation(hid1[:, n, :], ps_mlp[(MLP_OUTS * a + n) % 2][:, 0:HALF], ACT.Relu,
                                         bias=b1_sb[:, n:n + 1]).then_inc(mlp_copied, 1)
                v = HID1 // P
                for n in range(HID2 // P):
                    act.wait_ge(mlp_done, u + v + n + 1)
                    nc.scalar.activation(hid2[:, n, :], ps_mlp[(MLP_OUTS * a + v + n) % 2][:, 0:HALF], ACT.Relu,
                                         bias=b2_sb[:, n:n + 1]).then_inc(mlp_copied, 1)
                v += HID2 // P
                act.wait_ge(mlp_done, u + v + 1)
                nc.scalar.copy(y[:, bass.ds((2 * i + a) * HALF, HALF)],
                               ps_mlp[(MLP_OUTS * a + v) % 2][0:1, 0:HALF]).then_inc(mlp_copied, 1)

            act.wait_ge(pads_ready, 2)
            copy_features(act, copy, 0, 0, 0)
            copy_features(act, copy, 0, 0, 1)
            copy_products(act, copy, 0, 0, 0)
            copy_features(act, copy, 0, 0, 2)
            copy_products(act, copy, 0, 0, 1)
            act.wait_ge(weights_landed, 16 * 5)
            with act.Fori(0, LOOPS - 1) as i:
                copy_features(act, copy, 0, i, 3)
                copy_products(act, copy, 0, i, 2)
                mlp_results(i, 0)
                copy_features(act, copy, 0, i, 4)
                copy_products(act, copy, 0, i, 3)
                copy_features(act, copy, 0, i, 5)
                copy_products(act, copy, 0, i, 4)
                mlp_results(i, 1)
                copy_features(act, copy, 0, i, 6)
                copy_products(act, copy, 0, i, 5)
            last = LOOPS - 1
            copy_features(act, copy, 0, last, 3)
            copy_products(act, copy, 0, last, 2)
            mlp_results(last, 0)
            copy_products(act, copy, 0, last, 3)
            mlp_results(last, 1)

        @block.vector
        def _(dve):
            copy = nc.vector.tensor_copy

            def features(i, r):
                dve.wait_ge(turned, TURNS * (4 * i + r) + 1)
                h = r // 2
                dve.wait_ge(dense_landed[h % 2], 16 * (i + h // 2 + 1))
                copy(feat[r % 2][:, :, F - 1], dense_half[:, h % 2, P * (r % 2):P * (r % 2) + P]
                     ).then_inc(dense_copied, 1)
                copy_features(dve, copy, 1, i, r)

            nc.vector.memset(ident[:], 0.0).then_inc(ident_zero, 1)
            nc.vector.memset(nought[:], 0.0).then_inc(ident_zero, 1)
            for x in feat:
                nc.vector.memset(x[:, :, F:FPAD], 0.0).then_inc(pads_ready, 1)
            features(0, 0)
            features(0, 1)
            copy_products(dve, copy, 1, 0, 0)
            features(0, 2)
            copy_products(dve, copy, 1, 0, 1)
            with dve.Fori(0, LOOPS - 1) as i:
                features(i, 3)
                copy_products(dve, copy, 1, i, 2)
                features(i, 4)
                copy_products(dve, copy, 1, i, 3)
                features(i, 5)
                copy_products(dve, copy, 1, i, 4)
                features(i, 6)
                copy_products(dve, copy, 1, i, 5)
            last = LOOPS - 1
            features(last, 3)
            copy_products(dve, copy, 1, last, 2)
            copy_products(dve, copy, 1, last, 3)


def lay_out_w1(w1):
    w = np.zeros((4, FPAD, CHUNKS, HID1), w1.dtype)
    i, j = np.triu_indices(F, k=1)
    row = np.full((F, F), -1)
    row[i, j] = np.arange(len(i))
    for q in range(4):
        first = COL0[q] if q == 0 else COL0[q - 1] + COLS
        for c in range(COLS):
            g = COL0[q] + c
            if g >= first:
                w[q, :g, c] = w1[row[:g, g]]
    w = w.reshape(P, CHUNKS, HID1)
    w[:, COLS] = w1[len(i):]
    return w


def kernel(**inputs):
    import concourse.bacc as bacc
    from concourse.bass_utils import run_bass_kernel_spmd

    x = {k: np.asarray(v) for k, v in inputs.items()}
    dense = x["r_dense_x"]
    B = dense.shape[0]
    arrays = {"in_dense_t": np.ascontiguousarray(dense.T), "in_ids": x["ids"]}
    for f in range(TABLES):
        arrays[f"in_tbl_{f}"] = x[f"tbl_{f}"]
    arrays["in_w1"] = lay_out_w1(x["W_top1"])
    arrays["in_b1"] = np.ascontiguousarray(x["b_top1"].reshape(-1, P).T)
    arrays["in_w2"] = x["W_top2"]
    arrays["in_b2"] = np.ascontiguousarray(x["b_top2"].reshape(-1, P).T)
    arrays["in_w3"] = np.ascontiguousarray(x["W_top3"].reshape(-1, P).T)

    nc = bacc.Bacc("TRN2", target_bir_lowering=False, num_devices=1)
    aps = {k: nc.dram_tensor(k, a.shape, mybir.dt.from_np(a.dtype), kind="ExternalInput").ap()
           for k, a in arrays.items()}
    out = nc.dram_tensor("out_y", (B, 1), F32, kind="ExternalOutput").ap()
    bass_dlrm_tower(nc, aps["in_dense_t"], aps["in_ids"], [aps[f"in_tbl_{f}"] for f in range(TABLES)],
                    aps["in_w1"], aps["in_b1"], aps["in_w2"], aps["in_b2"], aps["in_w3"], out)
    r = run_bass_kernel_spmd(nc, [arrays], core_ids=[0])
    return r.results[0]["out_y"]
```

```python
from contextlib import ExitStack

import numpy as np

import concourse.bass as bass
from concourse import mybir

F32 = mybir.dt.float32
F32R = mybir.dt.float32r
I32 = mybir.dt.int32
ALU = mybir.AluOpType
ACT = mybir.ActivationFunctionType

P = 128
D = 128
TABLES = 26
F = TABLES + 1
FPAD = 32
HID1, HID2 = 512, 256
HALF = 2 * P

KEPT = 6
CHUNKS, VROWS = 8, 125
PAIRS = KEPT // 2
GATHERED = TABLES - KEPT
TURN = 4
TURNS = GATHERED // TURN
ROWS_IN = 16 * TURN

Z_COLS = [(1, 8), (9, 6), (15, 6), (21, 6)]
Z_WIDTH = 8
GROUP = 4
BATCH = 8
BATCHES = P // GROUP // BATCH

RECTS = [(0, 2, 3, 5), (0, 5, 3, 8), (1, 0, 3, 11), (1, 3, 3, 14), (2, 0, 3, 18), (2, 3, 3, 20),
         (3, 0, 3, 24), (3, 3, 3, 26), (0, 0, 2, 2)]
RECT_AT = [sum(r[3] for r in RECTS[:n]) for n in range(len(RECTS))]
ZP_ROWS = [P, P, RECT_AT[-1], D]
ZP_CHUNKS = len(ZP_ROWS)

USES = 4 * TURNS + 2 * PAIRS
TURN_USE = [2, 8, 15, 21]
PAIR_USE = [[0, 1, 7], [13, 14, 20]]
MLP_OUTS = HID1 // P + HID2 // P + 1


def turn_use(i, r):
    return TURN_USE[r % 4] + USES * (r // 4)


def pair_use(a, p):
    return PAIR_USE[a % 2][p] + USES * (a // 2)


def bass_dlrm_tower(nc, dense_t, ids_gathered, ids_kept, gathered, kept, w1, b1, w2, b2, w3, out):
    B = ids_gathered.shape[0]
    LOOPS = B // P // 4

    with ExitStack() as ctx:
        def sb(name, shape, dt=F32):
            return ctx.enter_context(nc.sbuf_tensor(name, shape, dt))

        def pb(name, shape):
            return ctx.enter_context(nc.psum_tensor(name, shape, F32))

        def sem(name):
            return ctx.enter_context(nc.semaphore(name))

        ident = sb("ident", [P, P])
        nought, turnstile = sb("nought", [P, 1]), sb("turnstile", [P, 4])
        row_int, row_no = sb("row_int", [P, CHUNKS], I32), sb("row_no", [P, CHUNKS])
        table_hi = sb("table_hi", [VROWS, KEPT, CHUNKS, D], F32R)
        table_lo = sb("table_lo", [VROWS, KEPT, CHUNKS, D], F32R)
        ids_now = sb("ids_now", [P, 4, GATHERED], I32)
        rows = sb("rows", [P, 4, GATHERED, D])
        ids_row = sb("ids_row", [P, 2, KEPT, HALF], I32)
        hot = sb("hot", [P, 2, CHUNKS, HALF], F32R)
        stage = [sb(f"stage{i}", [P, KEPT + 1, HALF]) for i in range(2)]
        feat = [sb(f"feat{i}", [P, P, FPAD]) for i in range(2)]
        z = [sb(f"z{i}", [P, Z_WIDTH, HALF]) for i in range(2)]
        zp = [sb(f"zp{i}", [P, ZP_CHUNKS, HALF]) for i in range(2)]
        w1_sb = sb("w1_sb", [P, ZP_CHUNKS, HID1])
        w2_sb = sb("w2_sb", [P, HID1 // P, HID2])
        w3_sb = sb("w3_sb", [P, HID2 // P])
        b1_sb = sb("b1_sb", [P, HID1 // P])
        b2_sb = sb("b2_sb", [P, HID2 // P])
        hid1 = sb("hid1", [P, HID1 // P, HALF])
        hid2 = sb("hid2", [P, HID2 // P, HALF])
        y = sb("y", [1, HALF])

        ps_feat = [pb(f"ps_feat{i}", [P, 512]) for i in range(2)]
        ps_gram = [pb(f"ps_gram{i}", [P, BATCH, P]) for i in range(2)]
        ps_mlp = [pb(f"ps_mlp{i}", [P, 512]) for i in range(2)]

        constants_set = sem("constants_set")
        ident_ready = sem("ident_ready")
        row_no_ready = sem("row_no_ready")
        pads_ready = sem("pads_ready")
        weights_landed = sem("weights_landed")
        table_landed = [sem(f"table_landed{n}") for n in range(KEPT)]
        hi_ready, lo_ready = sem("hi_ready"), sem("lo_ready")
        ids_landed = [sem(f"ids_landed{r}") for r in range(4)]
        rows_landed = [[sem(f"rows_landed{r}_{n}") for n in range(TURNS)] for r in range(4)]
        passed = sem("passed")
        ids_row_landed = [sem(f"ids_row_landed{a}") for a in range(2)]
        dense_landed = [sem(f"dense_landed{a}") for a in range(2)]
        hot_built = sem("hot_built")
        hot_used = sem("hot_used")
        turned = sem("turned")
        emptied = [sem("emptied0"), sem("emptied1")]
        staged_used = sem("staged_used")
        gram_done = sem("gram_done")
        z_copied = [sem("z_copied0"), sem("z_copied1")]
        packed = [sem("packed0"), sem("packed1")]
        mlp_done = sem("mlp_done")
        mlp_copied = sem("mlp_copied")
        y_written = sem("y_written")
        y_free = sem("y_free")

        block = ctx.enter_context(nc.Block())

        PACK_IN = 16 * (len(RECTS) + 1)

        def lent(n):
            if n < 4:
                return z[n // 2][0:VROWS, 4 * (n % 2):4 * (n % 2 + 1), :].rearrange("p c d -> p (c d)")
            return rows[0:VROWS, 3, CHUNKS * (n - 4):CHUNKS * (n - 3), :].rearrange("p c d -> p (c d)")

        @block.sync
        def _(sp):
            def load_ids(at, r):
                sp.dma_start(ids_now[:, r, :], ids_gathered[bass.ds(at, P), :]).then_inc(ids_landed[r], 16)

            def load_half(at, a):
                sp.dma_start(ids_row[:, a, :, :], ids_kept[:, bass.ds(at, HALF)].partition_broadcast(P)
                             ).then_inc(ids_row_landed[a], 16)

            def load_dense(at, a):
                sp.dma_start(stage[a][:, KEPT, :], dense_t[:, bass.ds(at, HALF)]).then_inc(dense_landed[a], 16)

            def pack(i, a):
                for e in range(2):
                    sp.wait_ge(z_copied[e], BATCHES // 2 * (4 * i + 2 * a + 2))
                for (q, c, width, height), at in zip(RECTS, RECT_AT):
                    sp.dma_start(zp[a][at:at + height, 0:width, :],
                                 z[a][FPAD * q:FPAD * q + height, c:c + width, :]).then_inc(packed[a], 16)
                sp.dma_start(zp[a][:, ZP_CHUNKS - 1, :], dense_t[:, bass.ds((2 * i + a) * HALF, HALF)]
                             ).then_inc(packed[a], 16)

            def load_table(n):
                sp.dma_start(lent(n), kept[n].rearrange("(p c) d -> p (c d)", c=CHUNKS)
                             ).then_inc(table_landed[n], 16)

            load_ids(0, 0)
            for n in range(4):
                load_table(n)
            load_half(0, 0)
            for n in range(4, KEPT):
                load_table(n)
            load_ids(P, 1)
            load_dense(0, 0)
            load_half(HALF, 1)
            load_ids(2 * P, 2)
            load_dense(HALF, 1)
            load_ids(3 * P, 3)
            sp.dma_start(w1_sb[:], w1).then_inc(weights_landed, 16)
            sp.dma_start(w2_sb[:], w2.rearrange("(k p) m -> p k m", p=P)).then_inc(weights_landed, 16)
            sp.dma_start(w3_sb[:], w3).then_inc(weights_landed, 16)
            sp.dma_start(b1_sb[:], b1).then_inc(weights_landed, 16)
            sp.dma_start(b2_sb[:], b2).then_inc(y_free, 16)
            with sp.Fori(0, LOOPS - 1) as i:
                for a in range(2):
                    sp.wait_ge(hot_built, KEPT * (2 * i + a + 1))
                    load_half((2 * i + a + 2) * HALF, a)
                    for r in range(2 * a, 2 * a + 2):
                        for n in range(TURNS):
                            sp.wait_ge(rows_landed[r][n], ROWS_IN * (i + 1))
                        load_ids((4 * i + r + 4) * P, r)
                    sp.wait_ge(staged_used, 2 * (2 * i + a + 1))
                    load_dense((2 * i + a + 2) * HALF, a)
                    pack(i, a)
            pack(LOOPS - 1, 0)
            pack(LOOPS - 1, 1)

        @block.gpsimd
        def _(pool):
            def gather(i, r):
                pool.wait_ge(ids_landed[r], 16 * (i + 1))
                nc.gpsimd.tensor_tensor(turnstile[:, r:r + 1], nought[:], nought[:], ALU.add).then_inc(passed, 1)
                for n in range(TURNS):
                    for f in range(TURN * n, TURN * (n + 1)):
                        nc.gpsimd.indirect_dma_start(
                            rows[:, r, f, :], None, gathered[f],
                            bass.IndirectOffsetOnAxis(ap=ids_now[:, r, f:f + 1], axis=0),
                        ).then_inc(rows_landed[r][n], 16)

            nc.gpsimd.iota(row_int[:], [[1, CHUNKS]], base=0, channel_multiplier=CHUNKS).then_inc(row_no_ready, 1)
            pool.wait_ge(constants_set, 2)
            nc.gpsimd.affine_select(out=ident[:], in_=ident[:], compare_op=ALU.not_equal, fill=1.0, base=0,
                                    pattern=[[-1, P]], channel_multiplier=1).then_inc(ident_ready, 1)
            for r in range(4):
                if r == 3:
                    pool.wait_ge(hi_ready, KEPT)
                    pool.wait_ge(lo_ready, KEPT)
                gather(0, r)
            with pool.Fori(1, LOOPS) as i:
                for r in range(4):
                    pool.wait_ge(turned, TURNS * (4 * i + r - 3))
                    pool.wait_ge(passed, 4 * i + r)
                    gather(i, r)

        def emptied_before(use, i, bank):
            return USES // 2 * i + (use - bank + 1) // 2

        @block.tensor
        def _(pe):
            def bank_free(use, i):
                if use >= 2 or not isinstance(i, int) or i > 0:
                    pe.wait_ge(emptied[use % 2], emptied_before(use, i, use % 2))

            def turn(i, r):
                for n in range(TURNS):
                    use = turn_use(i, r) + n
                    pe.wait_ge(rows_landed[r % 4][n], ROWS_IN * (i + r // 4 + 1))
                    bank_free(use, i)
                    for k in range(TURN):
                        mm = nc.tensor.transpose(ps_feat[use % 2][:, k * P:(k + 1) * P],
                                                 rows[:, r % 4, TURN * n + k, :], ident[:])
                    mm.then_inc(turned, 1)

            def look_up(i, a, p):
                use = pair_use(a, p)
                bank_free(use, i)
                for k in range(2):
                    pe.wait_ge(hot_built, KEPT * (2 * i + a) + 2 * p + k + 1)
                    for c in range(CHUNKS):
                        for table in (table_hi, table_lo):
                            mm = nc.tensor.matmul(ps_feat[use % 2][:, k * HALF:(k + 1) * HALF],
                                                  table[:, 2 * p + k, c, :], hot[0:VROWS, k, c, :],
                                                  start=(c == 0 and table is table_hi),
                                                  stop=(c == CHUNKS - 1 and table is table_lo))
                    mm.then_inc(hot_used, 1)

            def products(i, r):
                for e in range(2):
                    pe.wait_ge(emptied[e], emptied_before(turn_use(i, r) + TURNS, i, e))
                pe.wait_ge(staged_used, 4 * i + r + 1)
                x = feat[r % 2]
                for m in range(BATCHES):
                    b = BATCHES * r + m
                    if b >= 2 or not isinstance(i, int) or i > 0:
                        pe.wait_ge(z_copied[b % 2], BATCHES * 2 * i + b // 2)
                    for c in range(BATCH):
                        s = GROUP * (BATCH * m + c)
                        mm = nc.tensor.matmul(
                            ps_gram[b % 2][:, c, 0:GROUP * F],
                            x[:, s:s + GROUP, :].rearrange("d s f -> d (s f)"),
                            x[:, s:s + GROUP, 0:F], start=True, stop=True)
                    mm.then_inc(gram_done, 1)

            def mlp(i, a):
                pe.wait_ge(packed[a], PACK_IN * (i + 1))
                u = MLP_OUTS * a
                base = MLP_OUTS * 2 * i
                for n in range(HID1 // P):
                    if n >= 2:
                        pe.wait_ge(mlp_copied, base + u + n - 1)
                    for c, height in enumerate(ZP_ROWS):
                        mm = nc.tensor.matmul(ps_mlp[(u + n) % 2][:, 0:HALF], w1_sb[0:height, c, n * P:(n + 1) * P],
                                              zp[a][0:height, c, :], start=(c == 0), stop=(c == ZP_CHUNKS - 1))
                    mm.then_inc(mlp_done, 1)
                u += HID1 // P
                pe.wait_ge(mlp_copied, base + u)
                for n in range(HID2 // P):
                    for c in range(HID1 // P):
                        mm = nc.tensor.matmul(ps_mlp[(u + n) % 2][:, 0:HALF], w2_sb[:, c, n * P:(n + 1) * P],
                                              hid1[:, c, :], start=(c == 0), stop=(c == HID1 // P - 1))
                    mm.then_inc(mlp_done, 1)
                u += HID2 // P
                pe.wait_ge(mlp_copied, base + u)
                for c in range(HID2 // P):
                    mm = nc.tensor.matmul(ps_mlp[u % 2][0:1, 0:HALF], w3_sb[:, c:c + 1], hid2[:, c, :],
                                          start=(c == 0), stop=(c == HID2 // P - 1))
                mm.then_inc(mlp_done, 1)

            pe.wait_ge(ident_ready, 1)
            pe.wait_ge(hi_ready, KEPT)
            pe.wait_ge(lo_ready, KEPT)
            look_up(0, 0, 0)
            look_up(0, 0, 1)
            turn(0, 0)
            look_up(0, 0, 2)

            turn(0, 1)
            look_up(0, 1, 0)
            products(0, 0)
            look_up(0, 1, 1)
            turn(0, 2)
            look_up(0, 1, 2)
            products(0, 1)
            pe.wait_ge(weights_landed, 16 * 4)
            with pe.Fori(0, LOOPS - 1) as i:
                turn(i, 3)
                look_up(i, 2, 0)
                products(i, 2)
                look_up(i, 2, 1)
                turn(i, 4)
                look_up(i, 2, 2)
                products(i, 3)
                mlp(i, 0)

                turn(i, 5)
                look_up(i, 3, 0)
                products(i, 4)
                look_up(i, 3, 1)
                turn(i, 6)
                look_up(i, 3, 2)
                products(i, 5)
                mlp(i, 1)
            last = LOOPS - 1
            products(last, 2)
            mlp(last, 0)
            turn(last, 3)
            products(last, 3)
            mlp(last, 1)

        def copy_turned(eng, copy, ns, i, r):
            for n in ns:
                use = turn_use(i, r) + n
                eng.wait_ge(turned, TURNS * (4 * i + r) + n + 1)
                copy(feat[r % 2][:, :, TURN * n:TURN * (n + 1)].rearrange("d s f -> d f s"),
                     ps_feat[use % 2][:].rearrange("d (f s) -> d f s", f=TURN)).then_inc(emptied[use % 2], 1)

        def copy_products(eng, copy, ms, i, r):
            for m in ms:
                b = BATCHES * r + m
                eng.wait_ge(gram_done, BATCHES * 4 * i + b + 1)
                s = P * (r % 2) + GROUP * BATCH * m
                for j in range(GROUP):
                    for q, (g, width) in enumerate(Z_COLS):
                        at = F * j + g
                        last = copy(
                            z[r // 2 % 2][FPAD * q:FPAD * (q + 1), 0:width, s + j:s + GROUP * BATCH:GROUP],
                            ps_gram[b % 2][FPAD * j:FPAD * (j + 1), :, at:at + width].rearrange("p b c -> p c b"))
                last.then_inc(z_copied[b % 2], 1)

        ACT_TURNS, DVE_TURNS = [0, 2, 4], [1, 3]
        ACT_BATCHES, DVE_BATCHES = [0, 2], [1, 3]

        @block.scalar
        def _(act):
            copy = nc.scalar.copy

            def stage_pair(i, a, p):
                use = pair_use(a, p)
                act.wait_ge(hot_used, KEPT * (2 * i + a) + 2 * p + 2)
                if a >= 2:
                    act.wait_ge(staged_used, 2 * (2 * i + a - 1))
                copy(stage[a % 2][:, 2 * p:2 * p + 2, :], ps_feat[use % 2][:].rearrange("d (f s) -> d f s", f=2)
                     ).then_inc(emptied[use % 2], 1)

            def mlp_results(i, a):
                u = MLP_OUTS * (2 * i + a)
                for n in range(HID1 // P):
                    act.wait_ge(mlp_done, u + n + 1)
                    nc.scalar.activation(hid1[:, n, :], ps_mlp[(MLP_OUTS * a + n) % 2][:, 0:HALF], ACT.Relu,
                                         bias=b1_sb[:, n:n + 1]).then_inc(mlp_copied, 1)
                v = HID1 // P
                for n in range(HID2 // P):
                    act.wait_ge(mlp_done, u + v + n + 1)
                    nc.scalar.activation(hid2[:, n, :], ps_mlp[(MLP_OUTS * a + v + n) % 2][:, 0:HALF], ACT.Relu,
                                         bias=b2_sb[:, n:n + 1]).then_inc(mlp_copied, 1)
                v += HID2 // P
                act.wait_ge(mlp_done, u + v + 1)
                act.wait_ge(y_free, 16 * (2 * i + a + 1))
                copy(y[:], ps_mlp[(MLP_OUTS * a + v) % 2][0:1, 0:HALF]).then_inc(mlp_copied, 1)
                act.wait_ge(mlp_copied, u + v + 1)
                act.dma_start(out[bass.ds((2 * i + a) * HALF, HALF), :].rearrange("b o -> o b"), y[:]
                              ).then_inc(y_free, 16)

            for n in range(KEPT):
                act.wait_ge(table_landed[n], 16)
                copy(table_hi[:, n, :, :].rearrange("p c d -> p (c d)"), lent(n)).then_inc(hi_ready, 1)
            act.wait_ge(lo_ready, KEPT)
            act.wait_ge(pads_ready, 2)
            stage_pair(0, 0, 0)
            stage_pair(0, 0, 1)
            copy_turned(act, copy, ACT_TURNS, 0, 0)
            stage_pair(0, 0, 2)
            copy_turned(act, copy, ACT_TURNS, 0, 1)
            stage_pair(0, 1, 0)
            copy_products(act, copy, ACT_BATCHES, 0, 0)
            stage_pair(0, 1, 1)
            copy_turned(act, copy, ACT_TURNS, 0, 2)
            stage_pair(0, 1, 2)
            copy_products(act, copy, ACT_BATCHES, 0, 1)
            act.wait_ge(weights_landed, 16 * 4)
            with act.Fori(0, LOOPS - 1) as i:
                copy_turned(act, copy, ACT_TURNS, i, 3)
                stage_pair(i, 2, 0)
                copy_products(act, copy, ACT_BATCHES, i, 2)
                stage_pair(i, 2, 1)
                copy_turned(act, copy, ACT_TURNS, i, 4)
                stage_pair(i, 2, 2)
                copy_products(act, copy, ACT_BATCHES, i, 3)
                mlp_results(i, 0)

                copy_turned(act, copy, ACT_TURNS, i, 5)
                stage_pair(i, 3, 0)
                copy_products(act, copy, ACT_BATCHES, i, 4)
                stage_pair(i, 3, 1)
                copy_turned(act, copy, ACT_TURNS, i, 6)
                stage_pair(i, 3, 2)
                copy_products(act, copy, ACT_BATCHES, i, 5)
                mlp_results(i, 1)
            last = LOOPS - 1
            copy_products(act, copy, ACT_BATCHES, last, 2)
            mlp_results(last, 0)
            copy_turned(act, copy, ACT_TURNS, last, 3)
            copy_products(act, copy, ACT_BATCHES, last, 3)
            mlp_results(last, 1)
            act.wait_ge(y_free, 16 * (2 * LOOPS + 1))

        @block.vector
        def _(dve):
            copy = nc.vector.tensor_copy

            def build_pair(i, a, p):
                if p == 0:
                    dve.wait_ge(ids_row_landed[a % 2], 16 * (i + a // 2 + 1))
                for k in range(2):
                    if a > 0 or p > 0:
                        dve.wait_ge(hot_used, KEPT * (2 * i + a) + 2 * (p - 1) + k + 1)
                    for c in range(CHUNKS):
                        op = nc.vector.tensor_scalar(hot[0:VROWS, k, c, :], ids_row[0:VROWS, a % 2, 2 * p + k, :],
                                                     row_no[0:VROWS, c:c + 1], None, ALU.is_equal)
                    op.then_inc(hot_built, 1)

            def take_staged(i, r):
                h = r // 2
                for e in range(2):
                    dve.wait_ge(emptied[e], emptied_before(pair_use(h, PAIRS - 1) + 1, i, e))
                dve.wait_ge(dense_landed[h % 2], 16 * (i + h // 2 + 1))
                copy(feat[r % 2][:, :, GATHERED:F].rearrange("d s f -> d f s"),
                     stage[h % 2][:, :, P * (r % 2):P * (r % 2) + P]).then_inc(staged_used, 1)

            nc.vector.memset(ident[:], 0.0).then_inc(constants_set, 1)
            nc.vector.memset(nought[:], 0.0).then_inc(constants_set, 1)
            for x in feat:
                nc.vector.memset(x[:, :, F:FPAD], 0.0).then_inc(pads_ready, 1)
            dve.wait_ge(row_no_ready, 1)
            copy(row_no[:], row_int[:]).then_inc(row_no_ready, 1)
            for n in range(KEPT):
                dve.wait_ge(hi_ready, n + 1)
                nc.vector.tensor_tensor(table_lo[:, n, :, :].rearrange("p c d -> p (c d)"), lent(n),
                                        table_hi[:, n, :, :].rearrange("p c d -> p (c d)").bitcast(F32),
                                        ALU.subtract).then_inc(lo_ready, 1)
            dve.wait_ge(row_no_ready, 2)
            build_pair(0, 0, 0)
            build_pair(0, 0, 1)
            build_pair(0, 0, 2)
            copy_turned(dve, copy, DVE_TURNS, 0, 0)
            take_staged(0, 0)

            build_pair(0, 1, 0)
            copy_turned(dve, copy, DVE_TURNS, 0, 1)
            take_staged(0, 1)
            build_pair(0, 1, 1)
            copy_products(dve, copy, DVE_BATCHES, 0, 0)
            build_pair(0, 1, 2)
            copy_turned(dve, copy, DVE_TURNS, 0, 2)
            take_staged(0, 2)
            copy_products(dve, copy, DVE_BATCHES, 0, 1)
            with dve.Fori(0, LOOPS - 1) as i:
                for a in (1, 2):
                    build_pair(i, a + 1, 0)
                    copy_turned(dve, copy, DVE_TURNS, i, 2 * a + 1)
                    take_staged(i, 2 * a + 1)
                    build_pair(i, a + 1, 1)
                    copy_products(dve, copy, DVE_BATCHES, i, 2 * a)
                    build_pair(i, a + 1, 2)
                    copy_turned(dve, copy, DVE_TURNS, i, 2 * a + 2)
                    take_staged(i, 2 * a + 2)
                    copy_products(dve, copy, DVE_BATCHES, i, 2 * a + 1)
            last = LOOPS - 1
            copy_products(dve, copy, DVE_BATCHES, last, 2)
            copy_turned(dve, copy, DVE_TURNS, last, 3)
            take_staged(last, 3)
            copy_products(dve, copy, DVE_BATCHES, last, 3)


def lay_out_w1(w1, order):
    w = np.zeros((P, ZP_CHUNKS, w1.shape[1]), w1.dtype)
    i, j = np.triu_indices(F, k=1)
    row = np.full((F, F), -1)
    row[i, j] = row[j, i] = np.arange(len(i))
    for (q, first, width, height), at in zip(RECTS, RECT_AT):
        for c in range(width):
            g = Z_COLS[q][0] + first + c
            n = min(g, height)
            w[at:at + n, c] = w1[row[order[:n], order[g]]]
    w[:, ZP_CHUNKS - 1] = w1[len(i):]
    return w


def kernel(**inputs):
    import concourse.bacc as bacc
    from concourse.bass_utils import run_bass_kernel_spmd

    x = {k: np.asarray(v) for k, v in inputs.items()}
    tables = [x[f"tbl_{f}"] for f in range(TABLES)]
    kept = [f for f in range(TABLES) if len(tables[f]) == CHUNKS * VROWS][:KEPT]
    gathered = [f for f in range(TABLES) if f not in kept]
    order = np.array(gathered + kept + [TABLES])

    arrays = {"in_dense_t": np.ascontiguousarray(x["r_dense_x"].T)}
    arrays["in_ids_gathered"] = np.ascontiguousarray(x["ids"][:, gathered])
    arrays["in_ids_kept"] = np.ascontiguousarray(x["ids"][:, kept].T)
    for f in range(TABLES):
        arrays[f"in_tbl_{f}"] = tables[f]
    arrays["in_w1"] = lay_out_w1(x["W_top1"], order)
    arrays["in_b1"] = np.ascontiguousarray(x["b_top1"].reshape(-1, P).T)
    arrays["in_w2"] = x["W_top2"]
    arrays["in_b2"] = np.ascontiguousarray(x["b_top2"].reshape(-1, P).T)
    arrays["in_w3"] = np.ascontiguousarray(x["W_top3"].reshape(-1, P).T)

    nc = bacc.Bacc("TRN2", target_bir_lowering=False, num_devices=1)
    aps = {k: nc.dram_tensor(k, a.shape, mybir.dt.from_np(a.dtype), kind="ExternalInput").ap()
           for k, a in arrays.items()}
    out = nc.dram_tensor("out_y", (x["ids"].shape[0], 1), F32, kind="ExternalOutput").ap()
    bass_dlrm_tower(nc, aps["in_dense_t"], aps["in_ids_gathered"], aps["in_ids_kept"],
                    [aps[f"in_tbl_{f}"] for f in gathered], [aps[f"in_tbl_{f}"] for f in kept],
                    aps["in_w1"], aps["in_b1"], aps["in_w2"], aps["in_b2"], aps["in_w3"], out)
    r = run_bass_kernel_spmd(nc, [arrays], core_ids=[0])
    return r.results[0]["out_y"]
```

```python
from contextlib import ExitStack

import numpy as np

import concourse.bass as bass
from concourse import mybir

F32 = mybir.dt.float32
F32R = mybir.dt.float32r
I32 = mybir.dt.int32
ALU = mybir.AluOpType
ACT = mybir.ActivationFunctionType

P = 128
D = 128
TABLES = 26
F = TABLES + 1
FPAD = 32
HID1, HID2 = 512, 256
HALF = 2 * P

KEPT = 7
CHUNKS, VROWS = 8, 125
PAIRS = [range(n, min(n + 2, KEPT)) for n in range(0, KEPT, 2)]
GATHERED = TABLES - KEPT
GROUPS = [range(f, min(f + 4, GATHERED)) for f in range(0, GATHERED, 4)]
TURNS = len(GROUPS)

Z_COLS = [(1, 8), (9, 6), (15, 6), (21, 6)]
Z_WIDTH = 8
GROUP = 4
BATCH = 8
BATCHES = P // GROUP // BATCH

RECTS = [(0, 2, 3, 5), (0, 5, 3, 8), (1, 0, 3, 11), (1, 3, 3, 14), (2, 0, 3, 18), (2, 3, 3, 20),
         (3, 0, 3, 24), (3, 3, 3, 26), (0, 0, 2, 2)]
RECT_AT = [sum(r[3] for r in RECTS[:n]) for n in range(len(RECTS))]
ZP_CHUNKS = 4

HALF_USES = [("pair", 0), ("pair", 1), ("tile 0", 0), ("tile 0", 1), ("pair", 2), ("tile 0", 2),
             ("tile 0", 3), ("pair", 3), ("tile 0", 4)] + [("tile 1", n) for n in range(TURNS)]
MLP_OUTS = HID1 // P + HID2 // P + 1


def turn_use(r, n):
    return len(HALF_USES) * (r // 2) + HALF_USES.index((f"tile {r % 2}", n))


def pair_use(a, p):
    return len(HALF_USES) * a + HALF_USES.index(("pair", p))


def share(a, tile):
    return (a, slice(0, HALF)) if tile is None else (a + tile, slice(P * tile, P * (tile + 1)))


def bass_dlrm_tower(nc, dense_t, ids_gathered, ids_kept, gathered, kept, w1, b1, w2, b2, w3, out):
    B = ids_gathered.shape[0]
    LOOPS = B // P // 4

    with ExitStack() as ctx:
        def sb(name, shape, dt=F32):
            return ctx.enter_context(nc.sbuf_tensor(name, shape, dt))

        def pb(name, shape):
            return ctx.enter_context(nc.psum_tensor(name, shape, F32))

        def sem(name):
            return ctx.enter_context(nc.semaphore(name))

        ident = sb("ident", [P, P])
        nought, turnstile = sb("nought", [P, 1]), sb("turnstile", [P, 4])
        row_int, row_no = sb("row_int", [P, CHUNKS], I32), sb("row_no", [P, CHUNKS])
        table_hi = sb("table_hi", [VROWS, KEPT, CHUNKS, D], F32R)
        table_lo = sb("table_lo", [VROWS, KEPT, CHUNKS, D], F32R)
        ids_now = sb("ids_now", [P, 4, GATHERED], I32)
        rows = sb("rows", [P, 2, GATHERED, D])
        ids_row = sb("ids_row", [P, KEPT, HALF], I32)
        hot = sb("hot", [P, 2, CHUNKS, HALF], F32R)
        stage = sb("stage", [P, KEPT + 1, HALF])
        feat = [sb(f"feat{i}", [P, P, FPAD]) for i in range(2)]
        z = [sb(f"z{i}", [P, Z_WIDTH, HALF]) for i in range(2)]
        zp = sb("zp", [P, ZP_CHUNKS, HALF])
        zp_hi = sb("zp_hi", [P, ZP_CHUNKS, HALF], F32R)
        zp_lo = sb("zp_lo", [P, ZP_CHUNKS, HALF], F32R)
        w1_hi, w1_lo = (sb(f"w1_{x}", [P, ZP_CHUNKS, HID1], F32R) for x in ("hi", "lo"))
        w2_hi, w2_lo = (sb(f"w2_{x}", [P, HID1 // P, HID2], F32R) for x in ("hi", "lo"))
        w3_sb = sb("w3_sb", [P, HID2 // P])
        b1_sb = sb("b1_sb", [P, HID1 // P])
        b2_sb = sb("b2_sb", [P, HID2 // P])
        hid1 = sb("hid1", [P, HID1 // P, HALF])
        hid1_hi = sb("hid1_hi", [P, HID1 // P, HALF], F32R)
        hid1_lo = sb("hid1_lo", [P, HID1 // P, HALF], F32R)
        hid2 = sb("hid2", [P, HID2 // P, HALF])
        y = sb("y", [1, HALF])

        ps_feat = [pb(f"ps_feat{i}", [P, 512]) for i in range(2)]
        ps_gram = [pb(f"ps_gram{i}", [P, BATCH, P]) for i in range(2)]
        ps_mlp = [pb(f"ps_mlp{i}", [P, 512]) for i in range(2)]

        constants_set = sem("constants_set")
        ident_ready = sem("ident_ready")
        row_no_ready = sem("row_no_ready")
        pads_ready = sem("pads_ready")
        weights_landed = sem("weights_landed")
        table_landed = [sem(f"table_landed{n}") for n in range(KEPT)]
        hi_ready, lo_ready = sem("hi_ready"), sem("lo_ready")
        ids_landed = [sem(f"ids_landed{r}") for r in range(4)]
        rows_landed = [[sem(f"rows_landed{r}_{n}") for n in range(TURNS)] for r in range(4)]
        passed = sem("passed")
        ids_row_landed = sem("ids_row_landed")
        ids_last_landed = sem("ids_last_landed")
        dense_landed = sem("dense_landed")
        hot_built = sem("hot_built")
        hot_used = sem("hot_used")
        turned = sem("turned")
        emptied = [sem("emptied0"), sem("emptied1")]
        staged_used = sem("staged_used")
        gram_done = sem("gram_done")
        z_copied = [sem("z_copied0"), sem("z_copied1")]
        packed = [sem("packed0"), sem("packed1")]
        packed_last = sem("packed_last")
        packed_by_pool = sem("packed_by_pool")
        weights_hi = sem("weights_hi")
        weights_split = sem("weights_split")
        zp_free = sem("zp_free")
        zp_hi_ready = sem("zp_hi_ready")
        hid1_hi_ready, hid1_lo_ready = sem("hid1_hi_ready"), sem("hid1_lo_ready")
        mlp_done = sem("mlp_done")
        mlp_copied = sem("mlp_copied")
        y_free = sem("y_free")

        block = ctx.enter_context(nc.Block())

        PACK_IN = 16 * (len(RECTS) + 1)

        def lent(n):
            if n < 4:
                return z[n // 2][0:VROWS, 4 * (n % 2):4 * (n % 2 + 1), :].rearrange("p c d -> p (c d)")
            s = CHUNKS * D // FPAD
            return feat[1][0:VROWS, s * (n - 4):s * (n - 3), :].rearrange("p s f -> p (s f)")

        w1_lent = z[1][:].rearrange("p c d -> p (c d)")
        w2_lent = zp[:].rearrange("p c d -> p (c d)")

        def move_rects(eng, ns, a, cols, done):
            for n in ns:
                q, c, width, height = RECTS[n]
                eng.dma_start(zp[RECT_AT[n]:RECT_AT[n] + height, 0:width, cols],
                              z[a][FPAD * q:FPAD * q + height, c:c + width, cols]).then_inc(done, 16)

        RECTS_SP, RECTS_POOL = range(6), range(6, len(RECTS))

        @block.sync
        def _(sp):
            def load_ids(at, r):
                sp.dma_start(ids_now[:, r, :], ids_gathered[bass.ds(at, P), :]).then_inc(ids_landed[r], 16)

            def load_ids_row(at):
                sp.dma_start(ids_row[:, 0:KEPT - 1, :], ids_kept[0:KEPT - 1, bass.ds(at, HALF)].partition_broadcast(P)
                             ).then_inc(ids_row_landed, 16)

            def load_ids_last(at):
                sp.dma_start(ids_row[:, KEPT - 1:KEPT, :], ids_kept[KEPT - 1:KEPT, bass.ds(at, HALF)]
                             .partition_broadcast(P)).then_inc(ids_last_landed, 16)

            def load_dense(at):
                sp.dma_start(stage[:, KEPT, :], dense_t[:, bass.ds(at, HALF)]).then_inc(dense_landed, 16)

            def pack(i, a, tile=None):
                if tile != 1:
                    sp.wait_ge(zp_free, 2 * i + a + 1)
                    sp.dma_start(zp[:, ZP_CHUNKS - 1, :], dense_t[:, bass.ds((2 * i + a) * HALF, HALF)]
                                 ).then_inc(packed[a], 16)
                for e in range(2):
                    sp.wait_ge(z_copied[e], BATCHES * (4 * i + 2 * a + (2 if tile is None else tile + 1)))
                if tile == 1:
                    move_rects(sp, RECTS_SP, a, share(a, tile)[1], packed_last)
                else:
                    move_rects(sp, range(len(RECTS)), a, share(a, tile)[1], packed[a])

            def load_table(n):
                sp.dma_start(lent(n), kept[n].rearrange("(p c) d -> p (c d)", c=CHUNKS)
                             ).then_inc(table_landed[n], 16)

            load_ids(0, 0)
            load_ids_row(0)
            for n in range(KEPT):
                load_table(n)
            load_ids_last(0)
            for r in range(1, 4):
                load_ids(r * P, r)
            load_dense(0)
            sp.dma_start(w2_lent.rearrange("p (k m) -> p k m", m=HID2), w2.rearrange("(k p) m -> p k m", p=P)
                         ).then_inc(weights_landed, 16)
            sp.dma_start(w3_sb[:], w3).then_inc(weights_landed, 16)
            sp.dma_start(b1_sb[:], b1).then_inc(weights_landed, 16)
            sp.dma_start(b2_sb[:], b2).then_inc(y_free, 16)
            sp.wait_ge(lo_ready, 4)
            sp.dma_start(w1_lent, w1.rearrange("p c m -> p (c m)")).then_inc(weights_landed, 16)
            sp.wait_ge(hot_built, KEPT - 1)
            load_ids_row(HALF)
            sp.wait_ge(hot_built, KEPT)
            load_ids_last(HALF)
            with sp.Fori(0, LOOPS - 1) as i:
                for a in range(2):
                    sp.wait_ge(staged_used, 2 * (2 * i + a + 1))
                    load_dense((2 * i + a + 1) * HALF)
                    for r in range(2 * a, 2 * a + 2):
                        sp.wait_ge(turned, TURNS * (4 * i + r + 1))
                        load_ids((4 * i + r + 4) * P, r)
                    sp.wait_ge(hot_built, KEPT * (2 * i + a + 2) - 1)
                    load_ids_row((2 * i + a + 2) * HALF)
                    pack(i, a)
                    sp.wait_ge(hot_built, KEPT * (2 * i + a + 2))
                    load_ids_last((2 * i + a + 2) * HALF)
            sp.wait_ge(staged_used, 2 * (2 * LOOPS - 1))
            load_dense((2 * LOOPS - 1) * HALF)
            pack(LOOPS - 1, 0)
            pack(LOOPS - 1, 1, 0)
            pack(LOOPS - 1, 1, 1)

        @block.gpsimd
        def _(pool):
            def gather(i, r):
                pool.wait_ge(ids_landed[r], 16 * (i + 1))
                nc.gpsimd.tensor_tensor(turnstile[:, r:r + 1], nought[:], nought[:], ALU.add).then_inc(passed, 1)
                for n, group in enumerate(GROUPS):
                    for f in group:
                        nc.gpsimd.indirect_dma_start(
                            rows[:, r % 2, f, :], None, gathered[f],
                            bass.IndirectOffsetOnAxis(ap=ids_now[:, r, f:f + 1], axis=0),
                        ).then_inc(rows_landed[r][n], 16)

            nc.gpsimd.iota(row_int[:], [[1, CHUNKS]], base=0, channel_multiplier=CHUNKS).then_inc(row_no_ready, 1)
            pool.wait_ge(constants_set, 2)
            nc.gpsimd.affine_select(out=ident[:], in_=ident[:], compare_op=ALU.not_equal, fill=1.0, base=0,
                                    pattern=[[-1, P]], channel_multiplier=1).then_inc(ident_ready, 1)
            for r in range(4):
                if r >= 2:
                    pool.wait_ge(turned, TURNS * (r - 1))
                gather(0, r)
            with pool.Fori(1, LOOPS) as i:
                for r in range(4):
                    pool.wait_ge(turned, TURNS * (4 * i + r - 1))
                    pool.wait_ge(passed, 4 * i + r)
                    gather(i, r)
            pool.wait_ge(zp_free, 2 * LOOPS)
            for e in range(2):
                pool.wait_ge(z_copied[e], BATCHES * 4 * LOOPS)
            move_rects(nc.gpsimd, RECTS_POOL, 1, share(1, 1)[1], packed_by_pool)

        def emptied_before(use, i, bank):
            return len(HALF_USES) * i + (use - bank + 1) // 2

        @block.tensor
        def _(pe):
            def bank_free(use, i):
                if use >= 2 or not isinstance(i, int) or i > 0:
                    pe.wait_ge(emptied[use % 2], emptied_before(use, i, use % 2))

            def turn(i, r, ns):
                for n in ns:
                    use = turn_use(r, n)
                    pe.wait_ge(rows_landed[r % 4][n], 16 * len(GROUPS[n]) * (i + r // 4 + 1))
                    bank_free(use, i)
                    for k, f in enumerate(GROUPS[n]):
                        mm = nc.tensor.transpose(ps_feat[use % 2][:, k * P:(k + 1) * P],
                                                 rows[:, r % 2, f, :], ident[:])
                    mm.then_inc(turned, 1)

            def look_up(i, a, p):
                use = pair_use(a, p)
                bank_free(use, i)
                for k, n in enumerate(PAIRS[p]):
                    if isinstance(i, int) and a == 0:
                        pe.wait_ge(lo_ready, n + 1)
                    pe.wait_ge(hot_built, KEPT * (2 * i + a) + n + 1)
                    for c in range(CHUNKS):
                        for table in (table_hi, table_lo):
                            mm = nc.tensor.matmul(ps_feat[use % 2][:, k * HALF:(k + 1) * HALF],
                                                  table[:, n, c, :], hot[0:VROWS, (KEPT * a + n) % 2, c, :],
                                                  start=(c == 0 and table is table_hi),
                                                  stop=(c == CHUNKS - 1 and table is table_lo))
                    mm.then_inc(hot_used, 1)

            def products(i, r, ms):
                if isinstance(i, int) and r < 2:
                    pe.wait_ge(pads_ready, r + 1)
                if ms[0] == 0:
                    for e in range(2):
                        pe.wait_ge(emptied[e], emptied_before(turn_use(r, TURNS - 1) + 1, i, e))
                    pe.wait_ge(staged_used, 4 * i + r + 1)
                x = feat[r % 2]
                for m in ms:
                    b = BATCHES * r + m
                    if b >= 2 or not isinstance(i, int) or i > 0:
                        pe.wait_ge(z_copied[b % 2], 2 * (BATCHES * 2 * i + b // 2))
                    for c in range(BATCH):
                        s = GROUP * (BATCH * m + c)
                        mm = nc.tensor.matmul(
                            ps_gram[b % 2][:, c, 0:GROUP * F],
                            x[:, s:s + GROUP, :].rearrange("d s f -> d (s f)"),
                            x[:, s:s + GROUP, 0:F], start=True, stop=True)
                    mm.then_inc(gram_done, 1)

            def split_matmuls(result, w_hi, w_lo, x_hi, x_lo, n, chunks=range(ZP_CHUNKS)):
                terms = [(w, x) for w, x in ((w_hi, x_hi), (w_hi, x_lo), (w_lo, x_hi))]
                for c in chunks:
                    for k, (w, x) in enumerate(terms):
                        mm = nc.tensor.matmul(result, w[:, c, n * P:(n + 1) * P], x[:, c, :],
                                              start=(c == 0 and k == 0), stop=(c == ZP_CHUNKS - 1 and k == 2))
                if chunks[-1] == ZP_CHUNKS - 1:
                    mm.then_inc(mlp_done, 1)

            def layer1(i, a, ns, turns=1):
                if ns[0] == 0:
                    pe.wait_ge(zp_free, 2 * i + a + turns + 1)
                for n in ns:
                    if n >= 1:
                        pe.wait_ge(mlp_copied, MLP_OUTS * (2 * i + a) + n - 1)
                    split_matmuls(ps_mlp[(MLP_OUTS * a + n) % 2][:, 0:HALF], w1_hi, w1_lo, zp_hi, zp_lo, n)

            def layer2(i, a):
                pe.wait_ge(hid1_lo_ready, 2 * i + a + 1)
                for n in range(HID2 // P):
                    pe.wait_ge(mlp_copied, MLP_OUTS * (2 * i + a) + HID1 // P + n - 1)
                    split_matmuls(ps_mlp[(MLP_OUTS * a + HID1 // P + n) % 2][:, 0:HALF], w2_hi, w2_lo,
                                  hid1_hi, hid1_lo, n)

            def layer2_in_parts(i, a):
                split = 2 * i + a + (HID1 // P - 1) * a
                for chunks in (range(HID1 // P - 1), range(HID1 // P - 1, HID1 // P)):
                    for n in range(HID2 // P):
                        for c in chunks:
                            if n == 0:
                                pe.wait_ge(hid1_lo_ready, split + c + 1)
                            if c == 0:
                                pe.wait_ge(mlp_copied, MLP_OUTS * (2 * i + a) + HID1 // P + n - 1)
                            split_matmuls(ps_mlp[(MLP_OUTS * a + HID1 // P + n) % 2][:, 0:HALF], w2_hi, w2_lo,
                                          hid1_hi, hid1_lo, n, range(c, c + 1))

            def layer3(i, a):
                u = MLP_OUTS * a + MLP_OUTS - 1
                for c in range(HID2 // P):
                    pe.wait_ge(mlp_copied, MLP_OUTS * 2 * i + u + 1 - HID2 // P + c)
                    mm = nc.tensor.matmul(ps_mlp[u % 2][0:1, 0:HALF], w3_sb[:, c:c + 1], hid2[:, c, :],
                                          start=(c == 0), stop=(c == HID2 // P - 1))
                mm.then_inc(mlp_done, 1)

            def half(i, a, before):
                turn(i, 2 * a, [1])
                look_up(i, a, 2)
                turn(i, 2 * a, [2, 3])
                look_up(i, a, 3)
                turn(i, 2 * a, [4])
                products(i, 2 * a, [0, 1])
                if before:
                    layer1(i, a - 1, [0, 1])
                products(i, 2 * a, [2, 3])
                turn(i, 2 * a + 1, [0, 1])
                if before:
                    layer1(i, a - 1, [2])
                turn(i, 2 * a + 1, [2, 3])
                if before:
                    layer1(i, a - 1, [3])
                turn(i, 2 * a + 1, [4])
                look_up(i, a + 1, 0)
                products(i, 2 * a + 1, [0, 1])
                if before:
                    layer2(i, a - 1)
                look_up(i, a + 1, 1)
                if before:
                    layer3(i, a - 1)
                products(i, 2 * a + 1, [2])
                turn(i, 2 * a + 2, [0])
                products(i, 2 * a + 1, [3])

            pe.wait_ge(ident_ready, 1)
            look_up(0, 0, 0)
            look_up(0, 0, 1)
            turn(0, 0, [0])
            half(0, 0, False)
            pe.wait_ge(weights_split, 2)
            pe.wait_ge(weights_landed, 16 * 4)
            with pe.Fori(0, LOOPS - 1) as i:
                half(i, 1, True)
                half(i, 2, True)
            last = LOOPS - 1
            turn(last, 2, [1])
            look_up(last, 1, 2)
            turn(last, 2, [2, 3])
            look_up(last, 1, 3)
            turn(last, 2, [4])
            products(last, 2, [0, 1])
            turn(last, 3, [0, 1])
            products(last, 2, [2])
            turn(last, 3, [2])
            products(last, 2, [3])
            turn(last, 3, [3])
            layer1(last, 0, [0])
            turn(last, 3, [4])
            products(last, 3, range(BATCHES))
            layer1(last, 0, [1, 2, 3])
            layer2_in_parts(last, 0)
            layer3(last, 0)
            layer1(last, 1, [0, 1, 2, 3], turns=2)
            layer2_in_parts(last, 1)
            layer3(last, 1)

        ACT_PART, DVE_PART = (2, 3), (0, 1)

        def copy_products(eng, copy, js, ms, i, r):
            for m in ms:
                b = BATCHES * r + m
                eng.wait_ge(gram_done, BATCHES * 4 * i + b + 1)
                s = P * (r % 2) + GROUP * BATCH * m
                for j in js:
                    for q, (g, width) in enumerate(Z_COLS):
                        at = F * j + g
                        last = copy(
                            z[r // 2 % 2][FPAD * q:FPAD * (q + 1), 0:width, s + j:s + GROUP * BATCH:GROUP],
                            ps_gram[b % 2][FPAD * j:FPAD * (j + 1), :, at:at + width].rearrange("p b c -> p c b"))
                last.then_inc(z_copied[b % 2], 1)

        def copy_turned(eng, copy, ns, i, r):
            for n in ns:
                use = turn_use(r, n)
                eng.wait_ge(turned, TURNS * (4 * i + r) + n + 1)
                copy(feat[r % 2][:, :, GROUPS[n].start:GROUPS[n].stop].rearrange("d s f -> d f s"),
                     ps_feat[use % 2][:, 0:P * len(GROUPS[n])].rearrange("d (f s) -> d f s", s=P)
                      ).then_inc(emptied[use % 2], 1)

        @block.scalar
        def _(act):
            copy = nc.scalar.copy

            def stage_pair(i, a, p):
                use = pair_use(a, p)
                act.wait_ge(hot_used, KEPT * (2 * i + a) + PAIRS[p].stop)
                if a >= 1:
                    act.wait_ge(staged_used, 2 * (2 * i + a))
                copy(stage[:, PAIRS[p].start:PAIRS[p].stop, :],
                     ps_feat[use % 2][:, 0:HALF * len(PAIRS[p])].rearrange("d (f s) -> d f s", s=HALF)
                     ).then_inc(emptied[use % 2], 1)

            def split_zp(i, a, tile=None):
                run, cols = share(a, tile)
                if tile == 1:
                    act.wait_ge(packed_last, 16 * len(RECTS_SP))
                    act.wait_ge(packed_by_pool, 16 * len(RECTS_POOL))
                else:
                    act.wait_ge(packed[a % 2], PACK_IN * (i + a // 2 + 1))
                copy(zp_hi[:, :, cols], zp[:, :, cols]).then_inc(zp_hi_ready, 1)

            def split_hid1(i, a, n=None):
                ns = slice(0, HID1 // P) if n is None else slice(n, n + 1)
                act.wait_ge(mlp_copied, MLP_OUTS * (2 * i + a) + ns.stop)
                copy(hid1_hi[:, ns, :], hid1[:, ns, :]).then_inc(hid1_hi_ready, 1)

            def results(i, a, layer, ns):
                hid, bias, first = [(hid1, b1_sb, 0), (hid2, b2_sb, HID1 // P)][layer - 1]
                for n in ns:
                    act.wait_ge(mlp_done, MLP_OUTS * (2 * i + a) + first + n + 1)
                    nc.scalar.activation(hid[:, n, :], ps_mlp[(MLP_OUTS * a + first + n) % 2][:, 0:HALF],
                                         ACT.Relu, bias=bias[:, n:n + 1]).then_inc(mlp_copied, 1)

            def store_y(i, a):
                act.wait_ge(mlp_done, MLP_OUTS * (2 * i + a + 1))
                act.wait_ge(y_free, 16 * (2 * i + a + 1))
                copy(y[:], ps_mlp[(MLP_OUTS * a + MLP_OUTS - 1) % 2][0:1, 0:HALF]).then_inc(mlp_copied, 1)
                act.wait_ge(mlp_copied, MLP_OUTS * (2 * i + a + 1))
                act.dma_start(out[bass.ds((2 * i + a) * HALF, HALF), :].rearrange("b o -> o b"), y[:]
                              ).then_inc(y_free, 16)

            def half(i, a, before):
                copy_turned(act, copy, [1], i, 2 * a)
                stage_pair(i, a, 2)
                copy_turned(act, copy, [2, 3], i, 2 * a)
                stage_pair(i, a, 3)
                copy_turned(act, copy, [4], i, 2 * a)
                if before:
                    split_zp(i, a - 1)
                else:
                    act.wait_ge(lo_ready, KEPT)
                copy_products(act, copy, ACT_PART, [0, 1], i, 2 * a)
                if not before:
                    act.wait_ge(weights_landed, 16 * 4)
                    copy(w1_hi[:].rearrange("p c m -> p (c m)"), w1_lent).then_inc(weights_hi, 1)
                    copy(w2_hi[:].rearrange("p c m -> p (c m)"), w2_lent).then_inc(weights_hi, 1)
                if before:
                    results(i, a - 1, 1, [0, 1])
                copy_products(act, copy, ACT_PART, [2, 3], i, 2 * a)
                copy_turned(act, copy, [0, 1], i, 2 * a + 1)
                if before:
                    results(i, a - 1, 1, [2])
                copy_turned(act, copy, [2, 3], i, 2 * a + 1)
                if before:
                    results(i, a - 1, 1, [3])
                    split_hid1(i, a - 1)
                copy_turned(act, copy, [4], i, 2 * a + 1)
                stage_pair(i, a + 1, 0)
                copy_products(act, copy, ACT_PART, [0, 1], i, 2 * a + 1)
                if before:
                    results(i, a - 1, 2, [0, 1])
                stage_pair(i, a + 1, 1)
                if before:
                    store_y(i, a - 1)
                copy_products(act, copy, ACT_PART, [2], i, 2 * a + 1)
                copy_turned(act, copy, [0], i, 2 * a + 2)
                copy_products(act, copy, ACT_PART, [3], i, 2 * a + 1)

            for n in range(KEPT):
                act.wait_ge(table_landed[n], 16)
                copy(table_hi[:, n, :, :].rearrange("p c d -> p (c d)"), lent(n)).then_inc(hi_ready, 1)
            stage_pair(0, 0, 0)
            stage_pair(0, 0, 1)
            copy_turned(act, copy, [0], 0, 0)
            half(0, 0, False)
            act.wait_ge(weights_split, 2)
            with act.Fori(0, LOOPS - 1) as i:
                half(i, 1, True)
                half(i, 2, True)
            last = LOOPS - 1
            copy_turned(act, copy, [1], last, 2)
            stage_pair(last, 1, 2)
            copy_turned(act, copy, [2, 3], last, 2)
            stage_pair(last, 1, 3)
            copy_turned(act, copy, [4], last, 2)
            split_zp(last, 0)
            copy_products(act, copy, ACT_PART, [0, 1], last, 2)
            copy_turned(act, copy, [0, 1], last, 3)
            copy_products(act, copy, ACT_PART, [2, 3], last, 2)
            copy_turned(act, copy, [2, 3], last, 3)
            results(last, 0, 1, [0])
            split_hid1(last, 0, 0)
            copy_turned(act, copy, [4], last, 3)
            copy_products(act, copy, ACT_PART, range(BATCHES), last, 3)
            for n in range(1, HID1 // P):
                results(last, 0, 1, [n])
                split_hid1(last, 0, n)
            split_zp(last, 1, 0)
            results(last, 0, 2, [0, 1])
            split_zp(last, 1, 1)
            store_y(last, 0)
            for n in range(HID1 // P):
                results(last, 1, 1, [n])
                split_hid1(last, 1, n)
            results(last, 1, 2, [0, 1])
            store_y(last, 1)
            act.wait_ge(y_free, 16 * (2 * LOOPS + 1))

        @block.vector
        def _(dve):
            copy = nc.vector.tensor_copy

            def build(i, a, ns):
                if ns[0] == 0:
                    dve.wait_ge(ids_row_landed, 16 * (2 * i + a + 1))
                for n in ns:
                    if n == KEPT - 1:
                        dve.wait_ge(ids_last_landed, 16 * (2 * i + a + 1))
                    if a > 0 or n >= 2:
                        dve.wait_ge(hot_used, KEPT * (2 * i + a) + n - 1)
                    for c in range(CHUNKS):
                        op = nc.vector.tensor_scalar(hot[0:VROWS, (KEPT * a + n) % 2, c, :],
                                                     ids_row[0:VROWS, n, :],
                                                     row_no[0:VROWS, c:c + 1], None, ALU.is_equal)
                    op.then_inc(hot_built, 1)

            def take_staged(i, r):
                h = r // 2
                parts = [(0, KEPT + 1)] if r % 2 else [(0, KEPT - 1), (KEPT - 1, KEPT + 1)]
                for first, stop in parts:
                    pair = len(PAIRS) - (1 if stop > KEPT else 2)
                    for e in range(2):
                        dve.wait_ge(emptied[e], emptied_before(pair_use(h, pair) + 1, i, e))
                    if stop > KEPT:
                        dve.wait_ge(dense_landed, 16 * (2 * i + h + 1))
                    op = copy(feat[r % 2][:, :, GATHERED + first:GATHERED + stop].rearrange("d s f -> d f s"),
                              stage[:, first:stop, P * (r % 2):P * (r % 2) + P])
                op.then_inc(staged_used, 1)

            def rest(lo, x, hi, cols=slice(None)):
                return nc.vector.tensor_tensor(lo[:, :, cols], x, hi[:, :, cols].bitcast(F32), ALU.subtract)

            def rest_zp(i, a, tile=None):
                run, cols = share(a, tile)
                dve.wait_ge(zp_hi_ready, 2 * i + run + 1)
                rest(zp_lo, zp[:, :, cols], zp_hi, cols).then_inc(zp_free, 1)

            def rest_hid1(i, a, n=None):
                ns = slice(0, HID1 // P) if n is None else slice(n, n + 1)
                before = (HID1 // P - 1) * a if n is not None else 0
                dve.wait_ge(hid1_hi_ready, 2 * i + a + 1 + before + ns.start)
                rest(hid1_lo[:, ns, :], hid1[:, ns, :], hid1_hi[:, ns, :]).then_inc(hid1_lo_ready, 1)

            def half(i, a, before):
                build(i, a, [6])
                take_staged(i, 2 * a)
                if not before:
                    dve.wait_ge(lo_ready, KEPT)
                    nc.vector.memset(feat[1][:, :, F:FPAD], 0.0).then_inc(pads_ready, 1)
                take_staged(i, 2 * a + 1)
                if before:
                    rest_zp(i, a - 1)
                copy_products(dve, copy, DVE_PART, [0, 1], i, 2 * a)
                build(i, a + 1, [0, 1])
                copy_products(dve, copy, DVE_PART, [2, 3], i, 2 * a)
                if before:
                    rest_hid1(i, a - 1)
                else:
                    dve.wait_ge(weights_hi, 2)
                    rest(w1_lo, w1_lent.rearrange("p (c m) -> p c m", m=HID1), w1_hi).then_inc(weights_split, 1)
                    rest(w2_lo, w2_lent.rearrange("p (c m) -> p c m", m=HID2), w2_hi).then_inc(weights_split, 1)
                    dve.wait_ge(weights_split, 2)
                    nc.vector.memset(zp[P - 32:P, 2, :], 0.0).then_inc(zp_free, 1)
                build(i, a + 1, [2, 3])
                copy_products(dve, copy, DVE_PART, [0, 1], i, 2 * a + 1)
                build(i, a + 1, [4, 5])
                copy_products(dve, copy, DVE_PART, [2, 3], i, 2 * a + 1)

            nc.vector.memset(ident[:], 0.0).then_inc(constants_set, 1)
            nc.vector.memset(nought[:], 0.0).then_inc(constants_set, 1)
            nc.vector.memset(feat[0][:, :, F:FPAD], 0.0).then_inc(pads_ready, 1)
            dve.wait_ge(row_no_ready, 1)
            copy(row_no[:], row_int[:]).then_inc(row_no_ready, 1)
            dve.wait_ge(row_no_ready, 2)
            for n in range(KEPT):
                if n < KEPT - 1:
                    build(0, 0, [n])
                dve.wait_ge(hi_ready, n + 1)
                nc.vector.tensor_tensor(table_lo[:, n, :, :].rearrange("p c d -> p (c d)"), lent(n),
                                        table_hi[:, n, :, :].rearrange("p c d -> p (c d)").bitcast(F32),
                                        ALU.subtract).then_inc(lo_ready, 1)
            half(0, 0, False)
            with dve.Fori(0, LOOPS - 1) as i:
                half(i, 1, True)
                half(i, 2, True)
            last = LOOPS - 1
            build(last, 1, [6])
            take_staged(last, 2)
            take_staged(last, 3)
            rest_zp(last, 0)
            copy_products(dve, copy, DVE_PART, range(BATCHES), last, 2)
            copy_products(dve, copy, DVE_PART, range(BATCHES), last, 3)
            for n in range(HID1 // P):
                rest_hid1(last, 0, n)
            rest_zp(last, 1, 0)
            rest_zp(last, 1, 1)
            for n in range(HID1 // P):
                rest_hid1(last, 1, n)


def lay_out_w1(w1, order):
    w = np.zeros((P, ZP_CHUNKS, w1.shape[1]), w1.dtype)
    i, j = np.triu_indices(F, k=1)
    row = np.full((F, F), -1)
    row[i, j] = row[j, i] = np.arange(len(i))
    for (q, first, width, height), at in zip(RECTS, RECT_AT):
        for c in range(width):
            g = Z_COLS[q][0] + first + c
            n = min(g, height)
            w[at:at + n, c] = w1[row[order[:n], order[g]]]
    w[:, ZP_CHUNKS - 1] = w1[len(i):]
    return w


def kernel(**inputs):
    import concourse.bacc as bacc
    from concourse.bass_utils import run_bass_kernel_spmd

    x = {k: np.asarray(v) for k, v in inputs.items()}
    tables = [x[f"tbl_{f}"] for f in range(TABLES)]
    kept = [f for f in range(TABLES) if len(tables[f]) == CHUNKS * VROWS][:KEPT]
    gathered = [f for f in range(TABLES) if f not in kept]
    order = np.array(gathered + kept + [TABLES])

    arrays = {"in_dense_t": np.ascontiguousarray(x["r_dense_x"].T)}
    arrays["in_ids_gathered"] = np.ascontiguousarray(x["ids"][:, gathered])
    arrays["in_ids_kept"] = np.ascontiguousarray(x["ids"][:, kept].T)
    for f in range(TABLES):
        arrays[f"in_tbl_{f}"] = tables[f]
    arrays["in_w1"] = lay_out_w1(x["W_top1"], order)
    arrays["in_b1"] = np.ascontiguousarray(x["b_top1"].reshape(-1, P).T)
    arrays["in_w2"] = x["W_top2"]
    arrays["in_b2"] = np.ascontiguousarray(x["b_top2"].reshape(-1, P).T)
    arrays["in_w3"] = np.ascontiguousarray(x["W_top3"].reshape(-1, P).T)

    nc = bacc.Bacc("TRN2", target_bir_lowering=False, num_devices=1)
    aps = {k: nc.dram_tensor(k, a.shape, mybir.dt.from_np(a.dtype), kind="ExternalInput").ap()
           for k, a in arrays.items()}
    out = nc.dram_tensor("out_y", (x["ids"].shape[0], 1), F32, kind="ExternalOutput").ap()
    bass_dlrm_tower(nc, aps["in_dense_t"], aps["in_ids_gathered"], aps["in_ids_kept"],
                    [aps[f"in_tbl_{f}"] for f in gathered], [aps[f"in_tbl_{f}"] for f in kept],
                    aps["in_w1"], aps["in_b1"], aps["in_w2"], aps["in_b2"], aps["in_w3"], out)
    r = run_bass_kernel_spmd(nc, [arrays], core_ids=[0])
    return r.results[0]["out_y"]
```
